# Optimizing a Trainium2 kernel written in Bass

```python
import numpy as np
import jax
import jax.numpy as jnp

def _softmax(x, axis=-1):
    return jax.nn.softmax(x, axis=axis)
def _gelu(x):
    return jax.nn.gelu(x, approximate=True)
def _silu(x):
    return jax.nn.silu(x)
def _sigmoid(x):
    return jax.nn.sigmoid(x)
def _layernorm(x, axis=-1, eps=1e-5):
    m = jnp.mean(x, axis=axis, keepdims=True)
    v = jnp.var(x, axis=axis, keepdims=True)
    return (x - m) / jnp.sqrt(v + eps)
def _scatter_add(tgt, idx, src, axis=0):
    return tgt.at[idx].add(src)
def _segment_sum(src, seg, n):
    return jax.ops.segment_sum(src, seg, n)

kernel_name = 'mk_conv_preact_d1_conv_nchw768_fd60a1'

def setup_inputs(seed: int = 0):
    np.random.seed(seed)
    _w = jnp.asarray
    def _rec_inputs():
        import jax
        import jax.numpy as jnp
        _gk = jax.random.key(seed)
        x = -0.0001538 + 1 * jax.random.normal(jax.random.fold_in(_gk, 1), (8, 768, 32, 32), jnp.float32)
        return x
    x = _rec_inputs()
    def _L0_conv_setup():
        import jax, jax.numpy as jnp
        import numpy as np
        N_HEADS = 12
        D_EMBED = 768
        D_HEAD = D_EMBED // N_HEADS
        key = jax.random.key(seed)
        k1, k2, k3, k4, k5 = jax.random.split(key, 5)
        b, c, h, w = (8, D_EMBED, 32, 32)
        scale = 1.0 / np.sqrt(D_EMBED)
        return {'x': jax.random.normal(k1, (b, c, h, w), dtype=jnp.float32), 'in_proj_w': jax.random.normal(k2, (3 * D_EMBED, D_EMBED), dtype=jnp.float32) * scale, 'in_proj_b': jax.random.normal(k3, (3 * D_EMBED,), dtype=jnp.float32) * 0.02, 'out_proj_w': jax.random.normal(k4, (D_EMBED, D_EMBED), dtype=jnp.float32) * scale, 'out_proj_b': jax.random.normal(k5, (D_EMBED,), dtype=jnp.float32) * 0.02}
    _L0_conv_all = _L0_conv_setup()
    _L0_conv_in = {k: v for k, v in _L0_conv_all.items() if k in ('in_proj_w', 'in_proj_b', 'out_proj_w', 'out_proj_b', )}
    del _L0_conv_all

    return {
        "x": x,
        "L0_conv_in_proj_w": _L0_conv_in["in_proj_w"],
        "L0_conv_in_proj_b": _L0_conv_in["in_proj_b"],
        "L0_conv_out_proj_w": _L0_conv_in["out_proj_w"],
        "L0_conv_out_proj_b": _L0_conv_in["out_proj_b"],
    }

def reference(x, L0_conv_in_proj_w, L0_conv_in_proj_b, L0_conv_out_proj_w, L0_conv_out_proj_b):
    import jax
    import jax.numpy as jnp
    def _L0_conv_ref(x, in_proj_w, in_proj_b, out_proj_w, out_proj_b):
        import jax, jax.numpy as jnp
        import numpy as np
        N_HEADS = 12
        D_EMBED = 768
        D_HEAD = D_EMBED // N_HEADS
        b, c, h, w = x.shape
        s = h * w
        xs = x.reshape(b, c, s).transpose(0, 2, 1)
        qkv = xs @ in_proj_w.T + in_proj_b
        q, k, v = jnp.split(qkv, 3, axis=-1)
        q = q.reshape(b, s, N_HEADS, D_HEAD).transpose(0, 2, 1, 3)
        k = k.reshape(b, s, N_HEADS, D_HEAD).transpose(0, 2, 1, 3)
        v = v.reshape(b, s, N_HEADS, D_HEAD).transpose(0, 2, 1, 3)
        scores = jnp.einsum('bhqd,bhkd->bhqk', q, k) / jnp.sqrt(jnp.float32(D_HEAD))
        attn = jax.nn.softmax(scores, axis=-1)
        out = jnp.einsum('bhqk,bhkd->bhqd', attn, v)
        out = out.transpose(0, 2, 1, 3).reshape(b, s, c)
        out = out @ out_proj_w.T + out_proj_b
        return out.transpose(0, 2, 1).reshape(b, c, h, w)

    def _gn(v, G=32, eps=1e-5):
        B_, C_, H_, W_ = v.shape
        g = v.reshape(B_, G, C_ // G, H_, W_)
        m = jnp.mean(g, axis=(2, 3, 4), keepdims=True)
        s = jnp.var(g, axis=(2, 3, 4), keepdims=True)
        return ((g - m) / jnp.sqrt(s + eps)).reshape(v.shape)

    def _ln_c(v, eps=1e-6):
        m = jnp.mean(v, axis=1, keepdims=True)
        s = jnp.var(v, axis=1, keepdims=True)
        return (v - m) / jnp.sqrt(s + eps)

    def _ln_t(v, eps=1e-5):
        m = jnp.mean(v, axis=-1, keepdims=True)
        s = jnp.var(v, axis=-1, keepdims=True)
        return (v - m) / jnp.sqrt(s + eps)

    def _to_tokens(v):
        B_, C_, H_, W_ = v.shape
        return v.reshape(B_, C_, H_ * W_).transpose(0, 2, 1)
    def _from_tokens(t, like):
        B_, C_, H_, W_ = like.shape
        return t.transpose(0, 2, 1).reshape(B_, C_, H_, W_)

    x = x + _L0_conv_ref(_gn(x), L0_conv_in_proj_w, L0_conv_in_proj_b, L0_conv_out_proj_w, L0_conv_out_proj_b)
    return x


_drawn_inputs = setup_inputs


def setup_inputs(seed=0):
    import zlib

    import numpy as np

    out = dict(_drawn_inputs(seed))
    spreads = {}
    factors = {'L0_conv_in_proj_b': 2.841, 'L0_conv_out_proj_b': 2.783}
    for name, (base, spread) in spreads.items():
        noise = np.random.default_rng([zlib.crc32(name.encode()), seed]).standard_normal(out[name].shape)
        drawn = base * np.exp(spread * noise) if base else spread * noise
        out[name] = jnp.asarray(drawn.astype(out[name].dtype))
    for name, factor in factors.items():
        out[name] = (out[name] * factor).astype(out[name].dtype)
    return out
```

```python
from contextlib import ExitStack

import concourse.bass as bass
from concourse import mybir

F32 = mybir.dt.float32
F32R = mybir.dt.float32r
ALU = mybir.AluOpType
ACT = mybir.ActivationFunctionType
AX_X = mybir.AxisListType.X

P = 128
HALF = 512
D = 64
GROUPS = 32
GN_EPS = 1e-5
SCALE = 0.125



def conv_attention_kernel(nc, x, w_all, b_qkv, b_out, group_mean, out):
    B, C, S = x.shape
    CT = C // P
    PAIRS = C // P
    KT = S // P
    NH = S // HALF
    STEPS = 2 * KT
    LAG = 2
    PBUF = 4
    QKV = 3 * P
    WQ = CT * QKV
    WO = C
    MAX_TILES = [2, 1, 1, 1, 1, 1, 1, 0]
    assert S == NH * HALF and NH == 2 and sum(MAX_TILES) == KT and D * 2 == P

    w_hi_dram = nc.dram_tensor("w_hi_scratch", [PAIRS, P, WQ + WO], F32, kind="Internal").ap()
    w_lo_dram = nc.dram_tensor("w_lo_scratch", [PAIRS, P, WQ + WO], F32, kind="Internal").ap()
    x_dram = x.rearrange("b (p j) s -> b p j s", j=CT)
    out_dram = out.rearrange("b (p j) s -> b p j s", j=CT)

    with ExitStack() as ctx:
        def sb(name, shape, dt=F32):
            return ctx.enter_context(nc.sbuf_tensor(name, shape, dt))

        def sem(name):
            return ctx.enter_context(nc.semaphore(name))

        y = sb("y", [P, CT, S])
        xs = sb("xs", [P, 2, S])
        xh = sb("xh", [P, CT, S], F32R)
        xl = sb("xl", [P, CT, S], F32R)
        wqh = sb("wqh", [P, CT, QKV], F32R)
        wql = sb("wql", [P, CT, QKV], F32R)
        woh = sb("woh", [P, CT, P], F32R)
        wol = sb("wol", [P, CT, P], F32R)
        qa = sb("qa", [P, 2, S], F32R)
        ka = sb("ka", [P, 2, S], F32R)
        qb = sb("qb", [P, 2, S], F32R)
        kb = sb("kb", [P, 2, S], F32R)
        v = sb("v", [P, KT, 2, P], F32R)
        p_f = sb("p_f", [P, PBUF, S])
        p_h = sb("p_h", [P, 2, S], F32R)
        p_l = sb("p_l", [P, 2, S], F32R)
        psum_a = sb("psum_a", [P, S])
        psum_b = sb("psum_b", [P, S])
        o_bot = sb("o_bot", [P, HALF])
        o_sum = sb("o_sum", [P, HALF])
        o_rcp = sb("o_rcp", [P, HALF])
        o_n = sb("o_n", [P, S])
        oh = sb("oh", [P, S], F32R)
        ol = sb("ol", [P, S], F32R)
        mx = sb("mx", [P, 2, KT])
        ident = sb("ident", [P, P])
        ones = sb("ones", [P, D])
        bqkv = sb("bqkv", [P, PAIRS * 3])
        bout = sb("bout", [P, CT])
        gmean = sb("gmean", [P, P])
        st = sb("st", [P, CT * NH, 6])
        mv = sb("mv", [P, 2])
        gn = sb("gn", [P, 6])
        sums = [psum_a, psum_b]
        v_t = psum_b

        ps_s = ctx.enter_context(nc.psum_tensor("ps_s", [P, 2, S], F32))
        ps_m = ctx.enter_context(nc.psum_tensor("ps_m", [P, S], F32))
        ps_o = ctx.enter_context(nc.psum_tensor("ps_o", [P, S], F32))

        consts_in = sem("consts_in")
        w_raw_in = [sem(f"w_raw_in{i}") for i in range(2)]
        w_split_out = [sem(f"w_split_out{i}") for i in range(2)]
        wqkv_in = sem("wqkv_in")
        wout_in = sem("wout_in")
        y_in = sem("y_in")
        y_stored = sem("y_stored")
        xs_in = [sem(f"xs_in{i}") for i in range(2)]
        consts_set = sem("consts_set")
        w_hi_done = sem("w_hi_done")
        w_lo_done = sem("w_lo_done")
        stats_done = sem("stats_done")
        gn_step = sem("gn_step")
        gn_diff = sem("gn_diff")
        gn_mean = sem("gn_mean")
        gn_rstd = sem("gn_rstd")
        x_cent = sem("x_cent")
        x_hi = sem("x_hi")
        x_lo = sem("x_lo")
        q_proj = sem("q_proj")
        k_proj = sem("k_proj")
        v_proj = sem("v_proj")
        q_lo = sem("q_lo")
        q_dup = sem("q_dup")
        k_lo = sem("k_lo")
        k_dup = sem("k_dup")
        vt_done = sem("vt_done")
        v_turned = sem("v_turned")
        v_hi = sem("v_hi")
        v_lo = sem("v_lo")
        max_scores = [sem(f"max_scores{h}") for h in range(2)]
        max_taken = [sem(f"max_taken{h}") for h in range(2)]
        max_turned = [sem(f"max_turned{h}") for h in range(2)]
        max_row = [sem(f"max_row{h}") for h in range(2)]
        scores = sem("scores")
        p_done = sem("p_done")
        p_hi = sem("p_hi")
        p_lo = sem("p_lo")
        p_sum = sem("p_sum")
        pv = sem("pv")
        den = sem("den")
        rcp = sem("rcp")
        bot = sem("bot")
        o_added = sem("o_added")
        o_norm = sem("o_norm")
        o_hi = sem("o_hi")
        o_lo = sem("o_lo")
        y_proj = sem("y_proj")
        y_added = sem("y_added")

        block = ctx.enter_context(nc.Block())

        def loop(eng, body):
            with eng.Fori(0, B - 1) as b:
                with eng.Fori(0, PAIRS - 1) as pr:
                    body(b * PAIRS + pr, pr, b, False)
                body(b * PAIRS + PAIRS - 1, PAIRS - 1, b, True)
            with eng.Fori(0, PAIRS - 1) as pr:
                body((B - 1) * PAIRS + pr, pr, B - 1, False)
            body(B * PAIRS - 1, PAIRS - 1, B - 1, True)

        def has_next(b):
            return not (isinstance(b, int) and b == B - 1)

        @block.sync
        def _(sp):
            def load_slot(b, j, ring, waits=()):
                src = x_dram[b, :, j, :]
                if not isinstance(b, int):
                    sp.lower_val(src.offset * 4)
                for s, value in [(s, value if isinstance(value, int) else (sp.lower_val(value), value)[1]) for s, value in waits]:
                    sp.wait_ge(s, value)
                sp.dma_start(xs[:, ring, :], src).then_inc(xs_in[ring], 16)

            sp.dma_start(bqkv[:], b_qkv).then_inc(consts_in, 16)
            sp.dma_start(bout[:], b_out).then_inc(consts_in, 16)
            sp.dma_start(gmean[:], group_mean).then_inc(consts_in, 16)
            raw = [y[:, 3 * i:3 * i + 3, :].rearrange("p j s -> p (j s)") for i in range(2)]
            hi = [xh[:, 3 * i:3 * i + 3, :].rearrange("p j s -> p (j s)").bitcast(F32) for i in range(2)]
            lo = [xl[:, 3 * i:3 * i + 3, :].rearrange("p j s -> p (j s)").bitcast(F32) for i in range(2)]
            for i in range(PAIRS + 1):
                if i < PAIRS:
                    if i >= 2:
                        sp.wait_ge(w_lo_done, i - 1)
                    sp.dma_start(raw[i % 2], w_all[i]).then_inc(w_raw_in[i % 2], 16)
                if i >= 1:
                    sp.wait_ge(w_hi_done, i)
                    sp.wait_ge(w_lo_done, i)
                    sp.dma_start(w_hi_dram[i - 1], hi[(i - 1) % 2]).then_inc(w_split_out[(i - 1) % 2], 16)
                    sp.dma_start(w_lo_dram[i - 1], lo[(i - 1) % 2]).then_inc(w_split_out[(i - 1) % 2], 16)
            for i in range(2):
                sp.wait_ge(w_split_out[i], 32 * (PAIRS // 2))

            def load_wqkv(pair):
                sp.dma_start(wqh[:].bitcast(F32), w_hi_dram[pair, :, 0:WQ].rearrange("p (j n) -> p j n", j=CT)).then_inc(wqkv_in, 16)
                sp.dma_start(wql[:].bitcast(F32), w_lo_dram[pair, :, 0:WQ].rearrange("p (j n) -> p j n", j=CT)).then_inc(wqkv_in, 16)

            def load_wout(pair):
                sp.dma_start(woh[:].bitcast(F32), w_hi_dram[pair, :, WQ:WQ + WO].rearrange("p (j n) -> p j n", j=CT)).then_inc(wout_in, 16)
                sp.dma_start(wol[:].bitcast(F32), w_lo_dram[pair, :, WQ:WQ + WO].rearrange("p (j n) -> p j n", j=CT)).then_inc(wout_in, 16)

            def normalise_loads(b):
                for j in range(CT):
                    free = (x_lo, b * CT + j - 1) if j >= 2 else (stats_done, b * CT + CT)
                    load_slot(b, j, j % 2, [free])

            load_wqkv(0)
            load_wout(0)
            for j in range(CT):
                if j >= 1:
                    sp.wait_ge(stats_done, j)
                load_slot(0, j, 0)
            normalise_loads(0)

            def body(n, pair, b, last):
                if not last or has_next(b):
                    sp.wait_ge(v_proj, n + 1)
                    load_wqkv(0 if last else pair + 1)
                if has_next(b):
                    load_slot(b + 1, pair, 0, [(x_lo, (b + 1) * CT), (stats_done, n + CT)])
                if last and has_next(b):
                    normalise_loads(b + 1)
                if last:
                    sp.wait_ge(y_added, (n + 1) * CT)
                    sp.dma_start(out_dram[b], y[:]).then_inc(y_stored, 16)
                    if has_next(b):
                        sp.wait_ge(y_stored, (b + 1) * 16)
                        sp.dma_start(y[:], x_dram[b + 1]).then_inc(y_in, 16)
                if not last or has_next(b):
                    sp.wait_ge(y_proj, (n + 1) * CT)
                    load_wout(0 if last else pair + 1)

            sp.dma_start(y[:], x_dram[0]).then_inc(y_in, 16)
            loop(sp, body)
            sp.wait_ge(y_stored, 16 * B)

        @block.gpsimd
        def _(pool):
            nc.gpsimd.memset(ident[:], 0.0).then_inc(consts_set, 1)
            pool.wait_ge(consts_set, 1)
            nc.gpsimd.affine_select(out=ident[:], in_=ident[:], compare_op=ALU.not_equal, fill=1.0, base=0,
                                    pattern=[[-1, P]], channel_multiplier=1).then_inc(consts_set, 1)
            pool.wait_ge(consts_set, 2)
            nc.gpsimd.memset(ones[:], 1.0).then_inc(consts_set, 1)
            pool.wait_ge(consts_set, 3)
            nc.gpsimd.memset(gn[:, 5:6], -0.5).then_inc(consts_set, 1)
            pool.wait_ge(consts_set, 4)
            nc.gpsimd.memset(kb[D:D + 1, :, :].bitcast(F32), 1.0).then_inc(consts_set, 1)

            def rstd(b):
                pool.wait_ge(gn_step, b * 4 + 4)
                nc.gpsimd.tensor_tensor(gn[:, 4:5], gn[:, 3:4], gn[:, 5:6], ALU.pow).then_inc(gn_rstd, 1)

            pool.wait_ge(consts_set, 5)
            rstd(0)

            def body(n, pair, b, last):
                for h in range(2):
                    s = sums[h]
                    for t in range(1, KT):
                        g = h * KT + t
                        pool.wait_ge(p_done, n * STEPS + g + 1)
                        if t >= 2:
                            pool.wait_ge(p_sum, (n * 2 + h) * (KT - 1) + t - 1)
                        first = p_f[:, (g - 1) % PBUF, :] if t == 1 else s[:]
                        nc.gpsimd.tensor_tensor(s[:], first, p_f[:, g % PBUF, :], ALU.add).then_inc(p_sum, 1)
                        if h == 1 and t == 2 and last and has_next(b):
                            rstd(b + 1)

            loop(pool, body)

        @block.scalar
        def _(act):
            act.wait_ge(consts_in, 48)
            raw = [y[:, 3 * i:3 * i + 3, :] for i in range(2)]
            hi = [xh[:, 3 * i:3 * i + 3, :] for i in range(2)]
            for i in range(PAIRS):
                act.wait_ge(w_raw_in[i % 2], 16 * (i // 2 + 1))
                if i >= 2:
                    act.wait_ge(w_split_out[i % 2], 32 * (i // 2))
                nc.scalar.activation(hi[i % 2], raw[i % 2], ACT.Copy).then_inc(w_hi_done, 1)
            for i in range(2):
                act.wait_ge(w_split_out[i], 32 * (PAIRS // 2))

            def normalise_hi(b, j):
                act.wait_ge(x_cent, b * CT + j + 1)
                nc.scalar.activation(xh[:, j, :], xs[:, j % 2, :], ACT.Copy).then_inc(x_hi, 1)

            def evacuate_q(N, bias):
                act.wait_ge(q_proj, N + 1)
                for h in range(2):
                    rows = slice(D * h, D * h + D)
                    nc.scalar.activation(qa[0:D, h, :], ps_s[rows, 0, :], ACT.Identity, bias=bias[rows])
                    nc.scalar.activation(qa[D:P, h, :], ps_s[rows, 0, :], ACT.Identity, bias=bias[rows]).then_inc(q_dup, 1)

            def evacuate_k(N, bias):
                act.wait_ge(k_proj, N + 1)
                for h in range(2):
                    rows = slice(D * h, D * h + D)
                    nc.scalar.activation(ka[0:D, h, :], ps_s[rows, 1, :], ACT.Identity, bias=bias[rows])
                    nc.scalar.activation(kb[0:D, h, :], ps_s[rows, 1, :], ACT.Identity, bias=bias[rows]).then_inc(k_dup, 1)

            def max_to_row(count, h):
                act.wait_ge(max_turned[h], count + 1)
                nc.scalar.activation(qb[D:D + 1, h, :], ps_m[0:1, :], ACT.Copy, scale=-1.0).then_inc(max_row[h], 1)

            def evacuate_v(N, bias):
                act.wait_ge(v_proj, N + 1)
                nc.scalar.activation(v_t[:], ps_s[:, 0, :], ACT.Identity, bias=bias).then_inc(vt_done, 1)

            def v_high(N):
                act.wait_ge(v_turned, N + 1)
                nc.scalar.activation(v[:, :, :, 0:D], ps_s[:, 1, :].rearrange("p (t h d) -> p t h d", t=KT, h=2),
                                     ACT.Copy).then_inc(v_hi, 1)

            def move_bottom(n, h):
                act.wait_ge(pv, n * STEPS + h * KT + KT)
                for i in range(NH):
                    nc.scalar.activation(o_bot[D * i:D * i + D, :], ps_o[D:P, i * HALF:(i + 1) * HALF],
                                         ACT.Copy).then_inc(bot, 1)

            def bias_of(pair, which):
                c = pair * 3 + which
                return bqkv[:, c:c + 1] if isinstance(c, int) else bqkv[:, bass.ds(c, 1)]

            for j in range(CT):
                normalise_hi(0, j)
            evacuate_q(0, bias_of(0, 0))
            evacuate_k(0, bias_of(0, 1))
            evacuate_v(0, bias_of(0, 2))
            v_high(0)
            max_to_row(0, 0)

            def body(n, pair, b, last):
                norm = last and has_next(b)
                for g in range(STEPS):
                    act.wait_ge(scores, n * STEPS + g + 1)
                    if g >= PBUF:
                        act.wait_ge(p_lo, n * STEPS + g - PBUF + 1)
                        old = g - PBUF
                        adds = (old // KT) * (KT - 1) + max(old % KT, 1)
                        act.wait_ge(p_sum, n * 2 * (KT - 1) + adds)
                    nc.scalar.activation(p_f[:, g % PBUF, :], ps_s[:, g % 2, :], ACT.Exp, scale=SCALE).then_inc(p_done, 1)
                    if g >= 2:
                        act.wait_ge(pv, n * STEPS + g - 1)
                    nc.scalar.activation(p_h[:, g % 2, :], ps_s[:, g % 2, :], ACT.Exp, scale=SCALE).then_inc(p_hi, 1)
                    if g == KT - 2:
                        max_to_row(n, 1)
                    if g == KT + LAG - 1:
                        move_bottom(n, 0)
                    if norm and g >= KT + LAG + 1:
                        normalise_hi(b + 1, g - (KT + LAG + 1))
                nxt = (not last) or has_next(b)
                if norm:
                    for j in range(STEPS - (KT + LAG + 1), CT):
                        normalise_hi(b + 1, j)
                pair_next = 0 if last else pair + 1
                if nxt:
                    evacuate_q(n + 1, bias_of(pair_next, 0))
                move_bottom(n, 1)
                if nxt:
                    evacuate_k(n + 1, bias_of(pair_next, 1))
                act.wait_ge(o_norm, n * 4 + 4)
                nc.scalar.activation(oh[:], o_n[:], ACT.Copy).then_inc(o_hi, 1)
                if nxt:
                    evacuate_v(n + 1, bias_of(pair_next, 2))
                    v_high(n + 1)
                    max_to_row(n + 1, 0)

            loop(act, body)

        @block.vector
        def _(dve):
            raw = [y[:, 3 * i:3 * i + 3, :] for i in range(2)]
            hi = [xh[:, 3 * i:3 * i + 3, :].bitcast(F32) for i in range(2)]
            lo = [xl[:, 3 * i:3 * i + 3, :] for i in range(2)]
            for i in range(PAIRS):
                dve.wait_ge(w_hi_done, i + 1)
                if i >= 2:
                    dve.wait_ge(w_split_out[i % 2], 32 * (i // 2))
                nc.vector.tensor_tensor(lo[i % 2], raw[i % 2], hi[i % 2], ALU.subtract).then_inc(w_lo_done, 1)
            for i in range(2):
                dve.wait_ge(w_split_out[i], 32 * (PAIRS // 2))

            def slot_stats(b, j):
                dve.wait_ge(xs_in[0], (b * (CT + CT // 2) + j + 1) * 16)
                for i in range(NH):
                    c = j * NH + i
                    dst = st[:, c, :] if isinstance(c, int) else st[:, bass.ds(c, 1), :]
                    last = nc.vector.bn_stats(dst, xs[:, 0, i * HALF:(i + 1) * HALF])
                last.then_inc(stats_done, 1)

            def gn_first():
                nc.vector.bn_aggr(mv[:], st[:]).then_inc(gn_step, 1)

            def gn_second(b):
                dve.wait_ge(gn_mean, b * 2 + 1)
                nc.vector.tensor_copy(gn[:, 0:1], ps_m[:, 0:1]).then_inc(gn_step, 1)
                dve.wait_ge(gn_step, b * 4 + 2)
                nc.vector.tensor_tensor(gn[:, 1:2], mv[:, 0:1], gn[:, 0:1], ALU.subtract).then_inc(gn_diff, 1)
                dve.wait_ge(gn_diff, b + 1)
                nc.vector.scalar_tensor_tensor(gn[:, 2:3], gn[:, 1:2], gn[:, 1:2], mv[:, 1:2],
                                               ALU.mult, ALU.add).then_inc(gn_step, 1)

            def gn_third(b):
                dve.wait_ge(gn_mean, b * 2 + 2)
                nc.vector.tensor_scalar(gn[:, 3:4], ps_m[:, 0:1], GN_EPS, None, ALU.add).then_inc(gn_step, 1)

            def normalise(b, j):
                if isinstance(j, int) and j == 0:
                    dve.wait_ge(gn_rstd, b + 1)
                r = j % 2
                before = b * (CT + CT // 2) + CT if r == 0 else b * (CT // 2)
                dve.wait_ge(xs_in[r], (before + j // 2 + 1) * 16)
                nc.vector.tensor_scalar(xs[:, r, :], xs[:, r, :], gn[:, 0:1], gn[:, 4:5],
                                        ALU.subtract, ALU.mult).then_inc(x_cent, 1)
                dve.wait_ge(x_hi, b * CT + j + 1)
                nc.vector.tensor_tensor(xl[:, j, :], xs[:, r, :], xh[:, j, :].bitcast(F32), ALU.subtract).then_inc(x_lo, 1)

            def q_low(N, bias):
                for h in range(2):
                    dve.wait_ge(q_dup, 2 * N + h + 1)
                    rows = slice(D * h, D * h + D)
                    nc.vector.scalar_tensor_tensor(qb[0:D, h, :], ps_s[rows, 0, :], bias[rows], qa[0:D, h, :].bitcast(F32),
                                                   ALU.add, ALU.subtract).then_inc(q_lo, 1)

            def k_low(N, bias):
                for h in range(2):
                    dve.wait_ge(k_dup, 2 * N + h + 1)
                    rows = slice(D * h, D * h + D)
                    nc.vector.scalar_tensor_tensor(ka[D:P, h, :], ps_s[rows, 1, :], bias[rows], ka[0:D, h, :].bitcast(F32),
                                                   ALU.add, ALU.subtract).then_inc(k_lo, 1)

            def v_low(N):
                dve.wait_ge(v_hi, N + 1)
                nc.vector.tensor_tensor(v[:, :, :, D:P], ps_s[:, 1, :].rearrange("p (t h d) -> p t h d", t=KT, h=2),
                                        v[:, :, :, 0:D].bitcast(F32), ALU.subtract).then_inc(v_lo, 1)

            def take_max(count, h, t):
                dve.wait_ge(max_scores[h], count * KT + t + 1)
                nc.vector.tensor_reduce(mx[:, h, t:t + 1], ps_m[:], AX_X, ALU.max).then_inc(max_taken[h], 1)

            def reciprocal(n, h):
                dve.wait_ge(den, n * 2 + h + 1)
                nc.vector.reciprocal(o_rcp[:], ps_m[:, 0:HALF]).then_inc(rcp, 1)

            def add_bottom(n, h):
                dve.wait_ge(bot, (n * 2 + h) * 2 + 2)
                for i in range(NH):
                    nc.vector.tensor_tensor(o_sum[D * i:D * i + D, :], ps_o[0:D, i * HALF:(i + 1) * HALF],
                                            o_bot[D * i:D * i + D, :], ALU.add).then_inc(o_added, 1)

            def normalise_out(n, h):
                dve.wait_ge(rcp, n * 2 + h + 1)
                dve.wait_ge(o_added, (n * 2 + h) * 2 + 2)
                for i in range(NH):
                    nc.vector.tensor_tensor(o_n[D * h:D * h + D, i * HALF:(i + 1) * HALF], o_sum[D * i:D * i + D, :],
                                            o_rcp[D * i:D * i + D, :], ALU.mult).then_inc(o_norm, 1)

            def add_y(n, j, with_bias):
                dve.wait_ge(y_proj, n * CT + j + 1)
                if with_bias:
                    nc.vector.scalar_tensor_tensor(y[:, j, :], ps_s[:, j % 2, :], bout[:, j:j + 1], y[:, j, :],
                                                   ALU.add, ALU.add).then_inc(y_added, 1)
                else:
                    nc.vector.tensor_tensor(y[:, j, :], ps_s[:, j % 2, :], y[:, j, :], ALU.add).then_inc(y_added, 1)

            def bias_of(pair, which):
                c = pair * 3 + which
                return bqkv[:, c:c + 1] if isinstance(c, int) else bqkv[:, bass.ds(c, 1)]

            for j in range(CT):
                slot_stats(0, j)
            dve.wait_ge(stats_done, CT)
            gn_first()
            gn_second(0)
            gn_third(0)
            for j in range(CT):
                normalise(0, j)
            q_low(0, bias_of(0, 0))
            k_low(0, bias_of(0, 1))
            for t in range(KT):
                take_max(0, 0, t)
                if t == 2:
                    v_low(0)

            def body(n, pair, b, last):
                norm = last and has_next(b)
                taken = 0
                for g in range(STEPS):
                    if g < KT:
                        for _ in range(MAX_TILES[g]):
                            take_max(n, 1, taken)
                            taken += 1
                    if norm and g == 4:
                        dve.wait_ge(stats_done, (b + 2) * CT)
                    dve.wait_ge(p_hi, n * STEPS + g + 1)
                    if g >= 2:
                        dve.wait_ge(pv, n * STEPS + g - 1)
                    nc.vector.tensor_tensor(p_l[:, g % 2, :], p_f[:, g % PBUF, :], p_h[:, g % 2, :].bitcast(F32),
                                            ALU.subtract).then_inc(p_lo, 1)
                    if g == 3 and has_next(b):
                        slot_stats(b + 1, pair)
                    if norm:
                        if g == 4:
                            gn_first()
                        if g == KT:
                            gn_second(b + 1)
                        if g == KT + 1:
                            gn_third(b + 1)
                    if g == KT + LAG - 1:
                        add_bottom(n, 0)
                    if g == KT + LAG:
                        reciprocal(n, 0)
                        normalise_out(n, 0)
                    if norm and g >= KT + LAG + 1:
                        normalise(b + 1, g - (KT + LAG + 1))
                nxt = (not last) or has_next(b)
                pair_next = 0 if last else pair + 1
                if norm:
                    for j in range(STEPS - (KT + LAG + 1), CT):
                        normalise(b + 1, j)
                if nxt:
                    q_low(n + 1, bias_of(pair_next, 0))
                add_bottom(n, 1)
                if nxt:
                    k_low(n + 1, bias_of(pair_next, 1))
                reciprocal(n, 1)
                normalise_out(n, 1)
                dve.wait_ge(o_hi, n + 1)
                nc.vector.tensor_tensor(ol[:], o_n[:], oh[:].bitcast(F32), ALU.subtract).then_inc(o_lo, 1)
                if nxt:
                    take_max(n + 1, 0, 0)
                    take_max(n + 1, 0, 1)
                    v_low(n + 1)
                for j in range(CT):
                    if nxt:
                        take_max(n + 1, 0, j + 2)
                    if j == 0:
                        dve.wait_ge(y_in, b * 16 + 16)
                    add_y(n, j, last)

            loop(dve, body)

        @block.tensor
        def _(pe):
            pe.wait_ge(consts_set, 5)
            pe.wait_ge(consts_in, 48)

            def average(b, k):
                pe.wait_ge(gn_step, b * 4 + 2 * k + 1)
                col = mv[:, 0:1] if k == 0 else gn[:, 2:3]
                nc.tensor.matmul(ps_m[:, 0:1], gmean[:], col, start=True, stop=True).then_inc(gn_mean, 1)

            def project(N, which, buf, done, b, wait_x):
                w = slice(which * P, which * P + P)
                for j in range(CT):
                    if wait_x:
                        pe.wait_ge(x_lo, b * CT + j + 1)
                    for k, (ws, xx) in enumerate(((wqh, xh), (wqh, xl), (wql, xh))):
                        for i in range(NH):
                            last = nc.tensor.matmul(ps_s[:, buf, i * HALF:(i + 1) * HALF], ws[:, j, w],
                                                    xx[:, j, i * HALF:(i + 1) * HALF],
                                                    start=(j == 0 and k == 0), stop=(j == CT - 1 and k == 2))
                last.then_inc(done, 1)

            def max_scores_tile(count, h, t):
                for i in range(NH):
                    last = nc.tensor.matmul(ps_m[:, i * HALF:(i + 1) * HALF], qa[:, h, t * P:(t + 1) * P],
                                            ka[:, h, i * HALF:(i + 1) * HALF], start=True, stop=True)
                last.then_inc(max_scores[h], 1)

            def turn_max(count, h):
                pe.wait_ge(max_taken[h], (count + 1) * KT)
                for t in range(KT):
                    last = nc.tensor.transpose(ps_m[0:1, t * P:(t + 1) * P], mx[:, h, t:t + 1], ident[:])
                last.then_inc(max_turned[h], 1)

            def turn_v(N):
                pe.wait_ge(vt_done, N + 1)
                for t in range(KT):
                    last = nc.tensor.transpose(ps_s[:, 1, t * P:(t + 1) * P], v_t[:, t * P:(t + 1) * P], ident[:])
                last.then_inc(v_turned, 1)

            def denominator(n, h):
                pe.wait_ge(p_sum, (n * 2 + h + 1) * (KT - 1))
                for i in range(NH):
                    last = nc.tensor.matmul(ps_m[D * i:D * i + D, 0:HALF], ones[:],
                                            sums[h][:, i * HALF:(i + 1) * HALF], start=True, stop=True)
                last.then_inc(den, 1)

            def score_step(n, g):
                h, t = g // KT, g % KT
                if g >= 2:
                    pe.wait_ge(p_hi, n * STEPS + g - 1)
                if t == 0:
                    pe.wait_ge(max_row[h], n + 1)
                keys = slice(t * P, (t + 1) * P)
                for kk, qq, rows in ((ka, qa, P), (kb, qb, D + 1)):
                    for i in range(NH):
                        last = nc.tensor.matmul(ps_s[:, g % 2, i * HALF:(i + 1) * HALF], kk[0:rows, h, keys],
                                                qq[0:rows, h, i * HALF:(i + 1) * HALF],
                                                start=(rows == P), stop=(rows != P))
                last.then_inc(scores, 1)

            def value_step(n, g):
                h, t = g // KT, g % KT
                if g == KT:
                    pe.wait_ge(o_added, n * 4 + 2)
                pe.wait_ge(p_hi, n * STEPS + g + 1)
                for k, pp in enumerate((p_h, p_l)):
                    if k == 1:
                        pe.wait_ge(p_lo, n * STEPS + g + 1)
                    for i in range(NH):
                        last = nc.tensor.matmul(ps_o[:, i * HALF:(i + 1) * HALF], v[:, t, h, :],
                                                pp[:, g % 2, i * HALF:(i + 1) * HALF],
                                                start=(t == 0 and k == 0), stop=(t == KT - 1 and k == 1))
                last.then_inc(pv, 1)

            def wait_q_k(N):
                pe.wait_ge(q_dup, 2 * (N + 1))
                pe.wait_ge(q_lo, 2 * (N + 1))
                pe.wait_ge(k_dup, 2 * (N + 1))
                pe.wait_ge(k_lo, 2 * (N + 1))

            average(0, 0)
            average(0, 1)
            pe.wait_ge(wqkv_in, 32)
            project(0, 0, 0, q_proj, 0, True)
            project(0, 1, 1, k_proj, 0, False)
            pe.wait_ge(q_dup, 2)
            pe.wait_ge(q_lo, 2)
            project(0, 2, 0, v_proj, 0, False)
            wait_q_k(0)
            for t in range(KT):
                if t >= 1:
                    pe.wait_ge(max_taken[0], t)
                max_scores_tile(0, 0, t)
                if t == 1:
                    turn_v(0)
            turn_max(0, 0)

            def body(n, pair, b, last):
                norm = last and has_next(b)
                nxt = (not last) or has_next(b)
                pe.wait_ge(v_lo, n + 1)
                tile = 0
                for g in range(STEPS):
                    score_step(n, g)
                    if g < KT:
                        for _ in range(MAX_TILES[g]):
                            if tile >= 1:
                                pe.wait_ge(max_taken[1], n * KT + tile)
                            max_scores_tile(n, 1, tile)
                            tile += 1
                    if g == KT - 1:
                        turn_max(n, 1)
                    if norm and g == KT + 1:
                        average(b + 1, 0)
                    if norm and g == KT + 2:
                        average(b + 1, 1)
                    if g >= LAG:
                        value_step(n, g - LAG)
                    if g == KT + LAG:
                        if norm:
                            pe.wait_ge(gn_step, (b + 1) * 4 + 4)
                        denominator(n, 0)
                value_step(n, STEPS - 2)
                if nxt:
                    pe.wait_ge(p_hi, n * STEPS + STEPS - 1)
                    pe.wait_ge(wqkv_in, 32 * (n + 2))
                    project(n + 1, 0, 0, q_proj, b + 1, norm)
                value_step(n, STEPS - 1)
                if nxt:
                    project(n + 1, 1, 1, k_proj, b, False)
                pe.wait_ge(rcp, n * 2 + 1)
                denominator(n, 1)
                if nxt:
                    pe.wait_ge(q_dup, 2 * (n + 2))
                    pe.wait_ge(q_lo, 2 * (n + 2))
                    project(n + 1, 2, 0, v_proj, b, False)
                    wait_q_k(n + 1)
                    pe.wait_ge(rcp, n * 2 + 2)
                    max_scores_tile(n + 1, 0, 0)
                    pe.wait_ge(max_taken[0], (n + 1) * KT + 1)
                    max_scores_tile(n + 1, 0, 1)
                    turn_v(n + 1)
                pe.wait_ge(wout_in, 32 * (n + 1))
                pe.wait_ge(o_lo, n + 1)
                for j in range(CT):
                    if nxt:
                        pe.wait_ge(max_taken[0], (n + 1) * KT + j + 2)
                        max_scores_tile(n + 1, 0, j + 2)
                    if j == 1 and nxt:
                        pe.wait_ge(v_lo, n + 2)
                    if j >= 2:
                        pe.wait_ge(y_added, n * CT + j - 1)
                    for k, (ws, oo) in enumerate(((woh, oh), (woh, ol), (wol, oh))):
                        for i in range(NH):
                            mm = nc.tensor.matmul(ps_s[:, j % 2, i * HALF:(i + 1) * HALF], ws[:, j, :],
                                                  oo[:, i * HALF:(i + 1) * HALF], start=(k == 0), stop=(k == 2))
                    mm.then_inc(y_proj, 1)
                if nxt:
                    turn_max(n + 1, 0)
                pe.wait_ge(y_added, n * CT + CT)

            loop(pe, body)


def kernel(x, L0_conv_in_proj_w, L0_conv_in_proj_b, L0_conv_out_proj_w, L0_conv_out_proj_b):
    import numpy as np
    import concourse.bacc as bacc
    from concourse.bass_utils import run_bass_kernel_spmd

    x = np.asarray(x)
    B, C, H, W = x.shape
    S, CT, PAIRS = H * W, C // P, C // P
    w_in = np.asarray(L0_conv_in_proj_w).reshape(3, PAIRS, P, P, CT)
    w_in = w_in.transpose(1, 3, 4, 0, 2).reshape(PAIRS, P, CT * 3 * P)
    w_out = np.asarray(L0_conv_out_proj_w).reshape(P, CT, PAIRS, P)
    w_out = w_out.transpose(2, 3, 1, 0).reshape(PAIRS, P, CT * P)
    arrays = {
        "x_dram": np.ascontiguousarray(x.reshape(B, C, S)),
        "w_all_dram": np.ascontiguousarray(np.concatenate([w_in, w_out], axis=2)),
        "b_qkv_dram": np.ascontiguousarray(np.asarray(L0_conv_in_proj_b).reshape(3, PAIRS, P).transpose(2, 1, 0).reshape(P, PAIRS * 3)),
        "b_out_dram": np.ascontiguousarray(np.asarray(L0_conv_out_proj_b).reshape(P, CT)),
        "group_mean_dram": np.kron(np.eye(GROUPS), np.full((P // GROUPS, P // GROUPS), GROUPS / P)).astype(np.float32),
    }
    nc = bacc.Bacc("TRN2", target_bir_lowering=False, num_devices=1)
    args = [nc.dram_tensor(n, a.shape, mybir.dt.from_np(a.dtype), kind="ExternalInput").ap() for n, a in arrays.items()]
    out = nc.dram_tensor("out_dram", (B, C, S), F32, kind="ExternalOutput").ap()
    conv_attention_kernel(nc, *args, out)
    r = run_bass_kernel_spmd(nc, [arrays], core_ids=[0])
    return r.results[0]["out_dram"].reshape(B, C, H, W)
```

```python
from contextlib import ExitStack

import concourse.bass as bass
from concourse import mybir

F32 = mybir.dt.float32
F32R = mybir.dt.float32r
ALU = mybir.AluOpType
ACT = mybir.ActivationFunctionType
AX_X = mybir.AxisListType.X

P = 128
HALF = 512
D = 64
GROUPS = 32
GN_EPS = 1e-5
SIDES = 4
V_BANK, TURN_BANKS = 1, (2, 3)
SCALE = 0.125



def side_plan(kind, CT):
    def whole(name, *indices):
        return [(name, i, 0, CT) for i in indices]

    def slots(name, i, first, end):
        return [(name, i, first, end)]

    def mix(a, b):
        return [x for k in range(max(len(a), len(b))) for x in a[k:k + 1] + b[k:k + 1]]

    def out(*indices):
        return [] if kind == "start" else whole("out", *indices)

    last, later, more = kind == "last", kind != "start", kind != "final"
    plan = [
        whole("t", 0) + slots("qk", 0, 0, 3) + last * whole("avg", 0),
        slots("qk", 0, 3, CT) + later * whole("den", 1) + last * whole("avg", 1),
        slots("qk", 1, 0, 3) + whole("max", 0),
        slots("qk", 1, 3, CT) + whole("max", 2) + whole("t", 1),
        whole("max", 4, 6, 1, 3),
        mix(whole("max", 5, 7, 8, 9), out(0, 1, 2)),
        mix(whole("max", 10, 11, 12, 13), out(3, 4, 5)),
        whole("max", 14, 15) + out(6, 7) + whole("turn", 0, 1) + out(8),
        mix(more * slots("qk", 0, 0, 3), out(9, 10, 11)),
        more * slots("qk", 0, 3, CT) + whole("den", 0),
    ]
    if more:
        v = [[("v", i, j, j + 1) for j in range(CT)] for i in range(2)]
        plan += [
            slots("qk", 1, 0, 4) + whole("max", 0),
            slots("qk", 1, 4, CT) + whole("max", 2) + v[0][0:1] + whole("max", 4),
            mix(whole("max", 6, 1, 3, 5), v[0][1:4]),
            mix(whole("max", 7, 8, 9, 10), v[0][4:] + v[1][0:1]),
            mix(whole("max", 11, 12, 13, 14), v[1][1:3]),
            whole("max", 15) + v[1][3:5] + whole("turn", 0, 1) + v[1][5:],
        ]
    return plan + [[]] * (16 - len(plan))


def assign_banks(plan, CT):
    reading = {"qk": 3, "v": 1, "t": 1}
    banks, writing, free, at = {}, [False] * SIDES, [0] * SIDES, 0
    for g, step in enumerate(plan):
        for name, i, first, end in step:
            key = (name, i, g // 8 if name in ("qk", "max", "turn") else 0)
            if first == 0:
                bank = sorted((free[k], k) for k in range(SIDES) if not writing[k])[name == "avg"][1]
                banks[key], writing[bank] = bank, True
            if end == CT:
                writing[banks[key]] = False
            if name != "avg":
                at += 1
                free[banks[key]] = at + reading.get(name, 0)
    if ("v", 1, 0) in banks:
        part = max(key[2] for key in banks)
        number = {banks["turn", k, part]: TURN_BANKS[k] for k in range(2)}
        number.setdefault(banks["v", 1, 0], V_BANK)
        others = set(range(SIDES)) - set(number.values())
        number.update(zip(sorted(set(range(SIDES)) - set(number)), sorted(others)))
        banks = {key: number[bank] for key, bank in banks.items()}
    return banks


def ended(step, CT):
    return [(name, i) for name, i, _, end in step if end == CT]


def conv_attention_kernel(nc, x, w_all, b_qkv, b_out, group_mean, out):
    B, C, S = x.shape
    CT = C // P
    PAIRS = C // P
    KT = S // P
    NH = S // HALF
    STEPS = 2 * KT
    LAG = 2
    POOL_LOWS = (1, 2, 9, 10)
    UNIT = CT * P
    PARTS = PAIRS - 2
    PART = CT * NH // PARTS
    OUTS = CT * NH
    Y_RING = 4
    MAXES = KT * NH
    assert PART * PARTS == CT * NH and PART * HALF <= 2 * S
    assert S == NH * HALF and NH == 2 and D * 2 == P

    w_hi_dram = nc.dram_tensor("w_hi_scratch", [PAIRS * 4, P, UNIT], F32, kind="Internal").ap()
    w_lo_dram = nc.dram_tensor("w_lo_scratch", [PAIRS * 4, P, UNIT], F32, kind="Internal").ap()
    x_dram = x.rearrange("b (p j) s -> b p j s", j=CT)
    out_dram = out.rearrange("b (p j) s -> b p j s", j=CT)

    PROLOGUE = [[("avg", k) for k in range(2)], [("qk", i) for i in range(2)], [("v", i) for i in range(2)],
                [("max", i) for i in range(MAXES)], [("turn", i) for i in range(2)]]
    PLANS = {kind: side_plan(kind, CT) for kind in ("start", "loop", "last", "first", "final")}
    PLANS["prologue"] = [[(name, i, 0, CT) for tiles in PROLOGUE for name, i in tiles]]
    BANKS = {kind: assign_banks(plan, CT) for kind, plan in PLANS.items()}
    USES = {kind: [list(banks.values()).count(bank) for bank in range(SIDES)] for kind, banks in BANKS.items()}
    OUT_ORDER = [i for step in PLANS["loop"] for name, i in ended(step, CT) if name == "out"]

    BANKS["epilogue"] = {("den", 1, 0): 0, **{("out", i, 0): (k + 1) % SIDES for k, i in enumerate(OUT_ORDER)}}

    class Sides:

        def __init__(self, kind, base):
            self.kind, self.base, self.at = kind, base, [0] * SIDES

        def next(self, name, i, part=0):
            bank = BANKS[self.kind][name, i, part if name in ("qk", "max", "turn") else 0]
            self.at[bank] += 1
            return bank, self.base[bank] + (self.at[bank] - 1)

    def sides_of(n, b, kind):
        if kind == "prologue":
            return Sides(kind, [0] * SIDES)
        if kind == "start":
            return Sides(kind, USES["prologue"])
        more = [USES["last"][k] - USES["loop"][k] for k in range(SIDES)]
        base = [USES["prologue"][k] + USES["start"][k] + (n - 1) * USES["loop"][k] + b * more[k] for k in range(SIDES)]
        if kind == "epilogue":
            base = [base[k] - USES["loop"][k] + USES["final"][k] for k in range(SIDES)]
        return Sides(kind, base)

    with ExitStack() as ctx:
        def sb(name, shape, dt=F32):
            return ctx.enter_context(nc.sbuf_tensor(name, shape, dt))

        def sem(name):
            return ctx.enter_context(nc.semaphore(name))

        y = sb("y", [P, CT, S])
        xs = sb("xs", [P, 2, S])
        xh = sb("xh", [P, CT, S], F32R)
        xl = sb("xl", [P, CT, S], F32R)
        wqk = [sb(f"wqk_{x}", [P, CT, P], F32R) for x in ("h", "l")]
        wv = [sb(f"wv_{x}", [P, CT, P], F32R) for x in ("h", "l")]
        wo = [sb(f"wo_{x}", [P, CT, P], F32R) for x in ("h", "l")]
        qa = sb("qa", [P, 2, S], F32R)
        ka = sb("ka", [P, 2, S], F32R)
        qb = sb("qb", [P, 2, S], F32R)
        kb = sb("kb", [P, 2, S], F32R)
        v_t = sb("v_t", [P, S])
        v = sb("v", [P, KT, 2, P], F32R)
        p_f = sb("p_f", [P, 2, S])
        p_h = sb("p_h", [P, 2, S], F32R)
        p_l = sb("p_l", [P, 2, S], F32R)
        sums = sb("sums", [P, 2, S])
        o_bot = sb("o_bot", [P, HALF])
        o_sum = sb("o_sum", [P, HALF])
        o_rcp = sb("o_rcp", [P, HALF])
        o_n = sb("o_n", [P, S])
        oh = sb("oh", [P, S], F32R)
        ol = sb("ol", [P, S], F32R)
        y_part = sb("y_part", [P, Y_RING, HALF])
        mx = sb("mx", [P, NH, KT])
        mx_row = sb("mx_row", [P, KT])
        ident = sb("ident", [P, P])
        ones = sb("ones", [P, D])
        bqk = sb("bqk", [P, 2])
        bv = sb("bv", [P, 1])
        bout = sb("bout", [P, CT])
        gmean = sb("gmean", [P, P])
        st = sb("st", [P, CT * NH, 6])
        mv = sb("mv", [P, 2])
        g_mean = sb("g_mean", [P, 1])
        g_diff = sb("g_diff", [P, 1])
        g_sq = sb("g_sq", [P, 1])
        g_var = sb("g_var", [P, 1])
        g_rstd = sb("g_rstd", [P, 1])
        minus_half = sb("minus_half", [P, 1])

        ps_s = ctx.enter_context(nc.psum_tensor("ps_s", [P, S], F32))
        ps_o = ctx.enter_context(nc.psum_tensor("ps_o", [P, S], F32))
        side = [ctx.enter_context(nc.psum_tensor(f"side{k}", [P, HALF], F32)) for k in range(SIDES)]

        consts_in = sem("consts_in")
        w_raw_in = [sem(f"w_raw_in{i}") for i in range(2)]
        w_split_out = [sem(f"w_split_out{i}") for i in range(2)]
        wqk_in = sem("wqk_in")
        wv_in = sem("wv_in")
        wo_in = sem("wo_in")
        y_in = sem("y_in")
        y_stored = sem("y_stored")
        xs_in = [sem(f"xs_in{i}") for i in range(2)]
        part_in = sem("part_in")
        consts_set = sem("consts_set")
        w_hi_done = sem("w_hi_done")
        w_lo_done = sem("w_lo_done")
        side_ready = [sem(f"side_ready{k}") for k in range(SIDES)]
        side_free = [sem(f"side_free{k}") for k in range(SIDES)]
        stats_done = sem("stats_done")
        gn_step = sem("gn_step")
        gn_rstd = sem("gn_rstd")
        x_cent = sem("x_cent")
        x_hi = sem("x_hi")
        x_lo = sem("x_lo")
        qk_hi = sem("qk_hi")
        v_hi = sem("v_hi")
        max_done = sem("max_done")
        scores = sem("scores")
        p_done = sem("p_done")
        p_hi = sem("p_hi")
        p_lo = sem("p_lo")
        p_sum = sem("p_sum")
        pv = sem("pv")
        bot = sem("bot")
        o_added = sem("o_added")
        o_norm = sem("o_norm")
        o_hi = sem("o_hi")
        o_lo = sem("o_lo")
        y_added = sem("y_added")

        block = ctx.enter_context(nc.Block())

        def wait(eng, s, value):
            if not isinstance(value, int) or value > 0:
                eng.wait_ge(s, value)

        def loop(eng, body):
            body(0, 0, 0, "start")
            with eng.Fori(0, B - 1) as b:
                with eng.Fori(1, PAIRS - 1) as pr:
                    body(b * PAIRS + pr, pr, b, "loop")
                body(b * PAIRS + PAIRS - 1, PAIRS - 1, b, "last")
                body((b + 1) * PAIRS, 0, b + 1, "first")
            with eng.Fori(1, PAIRS - 1) as pr:
                body((B - 1) * PAIRS + pr, pr, B - 1, "loop")
            body(B * PAIRS - 1, PAIRS - 1, B - 1, "final")

        def next_pair(pair):
            return (pair + 1) % PAIRS if isinstance(pair, int) else pair + 1

        def probability_low(eng, ops, n, g):
            if g >= 1 and (g in POOL_LOWS) != (g - 1 in POOL_LOWS):
                eng.wait_ge(p_lo, n * STEPS + g)
            eng.wait_ge(p_hi, n * STEPS + g + 1)
            wait(eng, pv, n * STEPS + g - 1)
            ops.tensor_tensor(p_l[:, g % 2, :], p_f[:, g % 2, :], p_h[:, g % 2, :].bitcast(F32),
                              ALU.subtract).then_inc(p_lo, 1)

        @block.sync
        def _(sp):
            def load_slot(b, j, ring, waits=()):
                src = x_dram[b, :, j, :]
                if not isinstance(b, int):
                    sp.lower_val(src.offset * 4)
                for _, value in waits:
                    if not isinstance(value, int):
                        sp.lower_val(value)
                for s, value in waits:
                    sp.wait_ge(s, value)
                sp.dma_start(xs[:, ring, :], src).then_inc(xs_in[ring], 16)

            def load_unit(tiles, done, pair, which, waits=(), bias=None):
                u = pair * 4 + which
                pairs = [(t[:].bitcast(F32), d[u].rearrange("p (j n) -> p j n", j=CT))
                         for t, d in zip(tiles, (w_hi_dram, w_lo_dram))]
                if bias is not None:
                    pairs.append((bias, b_qkv[pair * 3 + which]))
                if not isinstance(u, int):
                    for _, src in pairs:
                        sp.lower_val(src.offset * 4)
                for _, value in waits:
                    if not isinstance(value, int):
                        sp.lower_val(value)
                for s, value in waits:
                    sp.wait_ge(s, value)
                for dst, src in pairs:
                    sp.dma_start(dst, src).then_inc(done, 16)

            sp.dma_start(bout[:], b_out).then_inc(consts_in, 16)
            sp.dma_start(gmean[:], group_mean).then_inc(consts_in, 16)
            third = CT // 2
            raw = [y[:, third * i:third * (i + 1), :].rearrange("p j s -> p (j s)") for i in range(2)]
            split = [[t[:, third * i:third * (i + 1), :].rearrange("p j s -> p (j s)").bitcast(F32).rearrange(
                "p (u n) -> p u n", u=4) for i in range(2)] for t in (xh, xl)]
            for i in range(PAIRS + 1):
                if i < PAIRS:
                    if i >= 2:
                        sp.wait_ge(w_lo_done, i - 1)
                    sp.dma_start(raw[i % 2], w_all[i]).then_inc(w_raw_in[i % 2], 16)
                    if i >= 2:
                        sp.wait_ge(stats_done, i - 1)
                    load_slot(0, i, i % 2)
                if i >= 1:
                    k = i - 1
                    sp.wait_ge(w_lo_done, i)
                    for d, t in ((w_hi_dram, split[0]), (w_lo_dram, split[1])):
                        sp.dma_start(d[4 * k:4 * k + 4].rearrange("u p n -> p u n"), t[k % 2]).then_inc(w_split_out[k % 2], 16)
            for i in range(2):
                sp.wait_ge(w_split_out[i], 32 * (PAIRS // 2))
            load_unit(wqk, wqk_in, 0, 0, bias=bqk[:, 0:1])
            load_unit(wv, wv_in, 0, 2, bias=bv[:])
            load_unit(wo, wo_in, 0, 3)
            for j in range(CT):
                load_slot(0, j, j % 2, [(stats_done, CT) if j < 2 else (x_lo, j - 1)])
            sp.dma_start(y[:], x_dram[0]).then_inc(y_in, 16)
            load_unit(wqk, wqk_in, 0, 1, [(qk_hi, 3)], bqk[:, 1:2])

            def body(n, pair, b, kind):
                q = next_pair(pair)
                nxt = kind != "final"
                if kind == "loop" and not (isinstance(b, int) and b == B - 1):
                    src = x_dram[b + 1].rearrange("p j s -> p (j s)")[:, bass.ds((pair - 1) * (PART * HALF), PART * HALF)]
                    sp.lower_val(src.offset * 4)
                    sp.lower_val((b + 1) * CT)
                    sp.lower_val(b * PARTS + pair + (CT - 1))
                    sp.wait_ge(x_lo, (b + 1) * CT)
                    sp.wait_ge(stats_done, b * PARTS + pair + (CT - 1))
                    sp.dma_start(xs[:].rearrange("p r s -> p (r s)")[:, 0:PART * HALF], src).then_inc(part_in, 16)
                if kind == "last":
                    for j in range(2):
                        load_slot(b + 1, j, j, [(stats_done, (b + 1) * PARTS + CT)])
                if nxt:
                    load_unit(wv, wv_in, q, 2, [(v_hi, 2 * n + 1)], bv[:])
                if nxt:
                    load_unit(wqk, wqk_in, q, 0, [(qk_hi, 8 * n + 7)], bqk[:, 0:1])
                if kind == "last":
                    for j in range(2, CT):
                        load_slot(b + 1, j, j % 2, [(x_lo, (b + 1) * CT + j - 1)])
                if kind == "first":
                    dst = out_dram[b - 1]
                    sp.lower_val(dst.offset * 4)
                    sp.wait_ge(y_added, n * OUTS)
                    sp.dma_start(dst, y[:]).then_inc(y_stored, 16)
                if kind != "start":
                    load_unit(wo, wo_in, pair, 3, [(y_added, n * OUTS)])
                if nxt:
                    load_unit(wqk, wqk_in, q, 1, [(qk_hi, 8 * n + 11)], bqk[:, 1:2])
                if kind == "first":
                    src = x_dram[b]
                    sp.lower_val(src.offset * 4)
                    sp.wait_ge(y_stored, b * 16)
                    sp.dma_start(y[:], src).then_inc(y_in, 16)

            loop(sp, body)
            sp.wait_ge(y_added, B * PAIRS * OUTS)
            sp.dma_start(out_dram[B - 1], y[:]).then_inc(y_stored, 16)
            sp.wait_ge(y_stored, 16 * B)

        @block.gpsimd
        def _(pool):
            nc.gpsimd.memset(ident[:], 0.0).then_inc(consts_set, 1)
            pool.wait_ge(consts_set, 1)
            nc.gpsimd.affine_select(out=ident[:], in_=ident[:], compare_op=ALU.not_equal, fill=1.0, base=0,
                                    pattern=[[-1, P]], channel_multiplier=1).then_inc(consts_set, 1)
            pool.wait_ge(consts_set, 2)
            nc.gpsimd.memset(ones[:], 1.0).then_inc(consts_set, 1)
            pool.wait_ge(consts_set, 3)
            nc.gpsimd.memset(minus_half[:], -0.5).then_inc(consts_set, 1)
            pool.wait_ge(consts_set, 4)
            nc.gpsimd.memset(kb[D:D + 1, :, :].bitcast(F32), 1.0).then_inc(consts_set, 1)
            pool.wait_ge(consts_set, 5)

            def read_side(sides, name, i, part, n, b):
                bank, used = sides.next(name, i, part)
                if name == "avg" and i == 1:
                    pool.wait_ge(side_free[bank], used + 1)
                    nc.gpsimd.tensor_tensor(g_rstd[:], g_var[:], minus_half[:], ALU.pow).then_inc(gn_rstd, 1)
                elif name == "out":
                    if i == OUT_ORDER[0]:
                        pool.wait_ge(y_in, 16 * (b + 1))
                    pool.wait_ge(side_free[bank], used + 1)
                    j, half = i // NH, slice((i % NH) * HALF, (i % NH + 1) * HALF)
                    nc.gpsimd.tensor_tensor(y[:, j, half], y[:, j, half], y_part[:, OUT_ORDER.index(i) % Y_RING, :],
                                            ALU.add).then_inc(y_added, 1)

            def out_low(n):
                pool.wait_ge(o_hi, n + 1)
                nc.gpsimd.tensor_tensor(ol[:], o_n[:], oh[:].bitcast(F32), ALU.subtract).then_inc(o_lo, 1)

            sides = sides_of(0, 0, "prologue")
            for tiles in PROLOGUE:
                for name, i in tiles:
                    read_side(sides, name, i, 0, 0, 0)

            def body(n, pair, b, kind):
                sides = sides_of(n, b, kind)
                for g, step in enumerate(PLANS[kind]):
                    h, t = g // KT, g % KT
                    if g - 1 in POOL_LOWS:
                        probability_low(pool, nc.gpsimd, n, g - 1)
                    if t >= 1:
                        pool.wait_ge(p_done, n * STEPS + g + 1)
                        if t == 1:
                            wait(pool, o_norm, 2 * n - 1 + h)
                        else:
                            pool.wait_ge(p_sum, (n * 2 + h) * (KT - 1) + t - 1)
                        first = p_f[:, (g - 1) % 2, :] if t == 1 else sums[:, h, :]
                        nc.gpsimd.tensor_tensor(sums[:, h, :], first, p_f[:, g % 2, :], ALU.add).then_inc(p_sum, 1)
                    if g == 4 and kind != "start":
                        out_low(n - 1)
                    for name, i in ended(step, CT):
                        read_side(sides, name, i, h, n - 1, b - 1 if kind == "first" else b)

            loop(pool, body)
            sides = sides_of(B * PAIRS, B - 1, "epilogue")
            sides.next("den", 1)
            out_low(B * PAIRS - 1)
            for i in OUT_ORDER:
                read_side(sides, "out", i, 0, B * PAIRS - 1, B - 1)

        @block.scalar
        def _(act):
            act.wait_ge(consts_in, 32)
            third = CT // 2
            for i in range(PAIRS):
                act.wait_ge(w_raw_in[i % 2], 16 * (i // 2 + 1))
                if i >= 2:
                    act.wait_ge(w_split_out[i % 2], 32 * (i // 2))
                part = slice(third * (i % 2), third * (i % 2 + 1))
                nc.scalar.activation(xh[:, part, :], y[:, part, :], ACT.Copy).then_inc(w_hi_done, 1)
            for i in range(2):
                act.wait_ge(w_split_out[i], 32 * (PAIRS // 2))

            def normalise_hi(b, j):
                act.wait_ge(x_cent, b * CT + j + 1)
                nc.scalar.activation(xh[:, j, :], xs[:, j % 2, :], ACT.Copy).then_inc(x_hi, 1)

            def read_side(sides, name, i, part, n, h, last_part):
                bank, used = sides.next(name, i, part)
                ps, half = side[bank], slice(i * HALF, (i + 1) * HALF)
                if name == "qk":
                    act.wait_ge(side_ready[bank], used + 1)
                    bias = bqk[:, h:h + 1]
                    for rows, first, second in ((slice(0, D), qa[0:D], qa[D:P]), (slice(D, P), ka[0:D], kb[0:D])):
                        nc.scalar.activation(first[:, h, half], ps[rows, :], ACT.Identity, bias=bias[rows])
                        nc.scalar.activation(second[:, h, half], ps[rows, :], ACT.Identity, bias=bias[rows]).then_inc(qk_hi, 1)
                elif name == "v":
                    act.wait_ge(side_ready[bank], used + 1)
                    nc.scalar.activation(v_t[:, half], ps[:], ACT.Identity, bias=bv[:]).then_inc(side_free[bank], 1)
                elif name == "t":
                    act.wait_ge(side_ready[bank], used + 1)
                    nc.scalar.activation(v[:, 4 * i:4 * i + 4, :, 0:D], ps[:].rearrange("p (t h d) -> p t h d", t=4, h=2),
                                         ACT.Copy).then_inc(v_hi, 1)
                elif name == "turn":
                    act.wait_ge(side_ready[bank], used + 1)
                    nc.scalar.activation(qb[D:D + 1, h, half], ps[0:1, :], ACT.Copy, scale=-1.0).then_inc(side_free[bank], 1)
                elif name == "out":
                    order = OUT_ORDER.index(i)
                    if order >= Y_RING:
                        act.wait_ge(y_added, n * OUTS + order + 1 - Y_RING)
                    act.wait_ge(side_ready[bank], used + 1)
                    bias = bout[:, i // NH:i // NH + 1] if last_part else 0.0
                    nc.scalar.activation(y_part[:, order % Y_RING, :], ps[:], ACT.Identity, bias=bias).then_inc(side_free[bank], 1)

            def move_bottom(n, h):
                act.wait_ge(pv, n * STEPS + h * KT + KT)
                for i in range(NH):
                    last = nc.scalar.activation(o_bot[D * i:D * i + D, :], ps_o[D:P, i * HALF:(i + 1) * HALF], ACT.Copy)
                last.then_inc(bot, 1)

            def out_high(n):
                act.wait_ge(o_norm, 2 * n + 2)
                nc.scalar.activation(oh[:], o_n[:], ACT.Copy).then_inc(o_hi, 1)

            sides = sides_of(0, 0, "prologue")
            for tiles in PROLOGUE:
                for name, i in tiles:
                    read_side(sides, name, i, 0, 0, 0, False)
                if tiles[0][0] == "avg":
                    for j in range(CT):
                        normalise_hi(0, j)

            def body(n, pair, b, kind):
                sides = sides_of(n, b, kind)

                def read_step(g, step):
                    for name, i in ended(step, CT):
                        ahead = name == "v" or g >= KT
                        read_side(sides, name, i, g // KT, n - 1 if name == "out" else n, 0 if ahead else 1, kind == "first")

                for g, step in enumerate(PLANS[kind]):
                    act.wait_ge(scores, n * STEPS + g + 1)
                    wait(act, p_lo, n * STEPS + g - 1)
                    wait(act, p_sum, n * 2 * (KT - 1) + ((g - 2) // KT) * (KT - 1) + max((g - 2) % KT, 1))
                    nc.scalar.activation(p_f[:, g % 2, :], ps_s[:], ACT.Exp, scale=SCALE).then_inc(p_done, 1)
                    if g == 1 and kind != "start":
                        move_bottom(n - 1, 1)
                    if g == KT + 1:
                        move_bottom(n, 0)
                    wait(act, pv, n * STEPS + g - 1)
                    nc.scalar.activation(p_h[:, g % 2, :], ps_s[:], ACT.Exp, scale=SCALE).then_inc(p_hi, 1)
                    if kind == "last" and 3 < g < 3 + CT:
                        normalise_hi(b + 1, g - 3)
                    read_step(g, step)
                    if kind == "last" and g == 3:
                        normalise_hi(b + 1, 0)
                    if g == 3 and kind != "start":
                        out_high(n - 1)

            loop(act, body)
            n = B * PAIRS
            sides = sides_of(n, B - 1, "epilogue")
            sides.next("den", 1)
            move_bottom(n - 1, 1)
            out_high(n - 1)
            for i in OUT_ORDER:
                read_side(sides, "out", i, 0, n - 1, 1, True)

        @block.vector
        def _(dve):
            def slot_statistics(b, j, ring, loads):
                dve.wait_ge(xs_in[ring], loads * 16)
                for i in range(NH):
                    c = j * NH + i
                    dst = st[:, c, :] if isinstance(c, int) else st[:, bass.ds(c, 1), :]
                    last = nc.vector.bn_stats(dst, xs[:, ring, i * HALF:(i + 1) * HALF])
                last.then_inc(stats_done, 1)

            def part_statistics(b, part):
                dve.wait_ge(part_in, ((b - 1) * PARTS + part + 1) * 16)
                for k in range(PART):
                    last = nc.vector.bn_stats(st[:, bass.ds(part * PART + k, 1), :],
                                              xs[:].rearrange("p r s -> p (r s)")[:, k * HALF:(k + 1) * HALF])
                last.then_inc(stats_done, 1)

            def centre(b, j):
                if j == 0:
                    dve.wait_ge(gn_rstd, b + 1)
                dve.wait_ge(xs_in[j % 2], (CT // 2 * (b + 1) + j // 2 + 1) * 16)
                x_slot = xs[:, j % 2, :]
                nc.vector.tensor_scalar(x_slot, x_slot, g_mean[:], g_rstd[:], ALU.subtract, ALU.mult).then_inc(x_cent, 1)

            def normalise_lo(b, j):
                dve.wait_ge(x_hi, b * CT + j + 1)
                nc.vector.tensor_tensor(xl[:, j, :], xs[:, j % 2, :], xh[:, j, :].bitcast(F32), ALU.subtract).then_inc(x_lo, 1)

            def read_side(sides, name, i, part, n, h, b):
                bank, used = sides.next(name, i, part)
                ps, half = side[bank], slice(i * HALF, (i + 1) * HALF)
                if name == "qk":
                    tile = (2 * n + h) * NH + i
                    bias = bqk[:, h:h + 1]
                    dve.wait_ge(qk_hi, 2 * tile + 1)
                    nc.vector.scalar_tensor_tensor(qb[0:D, h, half], ps[0:D, :], bias[0:D], qa[0:D, h, half].bitcast(F32),
                                                   ALU.add, ALU.subtract)
                    dve.wait_ge(qk_hi, 2 * tile + 2)
                    nc.vector.scalar_tensor_tensor(ka[D:P, h, half], ps[D:P, :], bias[D:P], ka[0:D, h, half].bitcast(F32),
                                                   ALU.add, ALU.subtract).then_inc(side_free[bank], 1)
                elif name == "t":
                    dve.wait_ge(v_hi, n * NH + i + 1)
                    nc.vector.tensor_tensor(v[:, 4 * i:4 * i + 4, :, D:P], ps[:].rearrange("p (t h d) -> p t h d", t=4, h=2),
                                            v[:, 4 * i:4 * i + 4, :, 0:D].bitcast(F32), ALU.subtract).then_inc(side_free[bank], 1)
                elif name == "max":
                    dve.wait_ge(side_ready[bank], used + 1)
                    nc.vector.tensor_reduce(mx[:, i % NH, i // NH:i // NH + 1], ps[:], AX_X, ALU.max).then_inc(side_free[bank], 1)
                    if i == MAXES - 1:
                        dve.wait_ge(side_free[bank], used + 1)
                        nc.vector.tensor_tensor(mx_row[:], mx[:, 0, :], mx[:, 1, :], ALU.max).then_inc(max_done, 1)
                elif name == "den":
                    dve.wait_ge(side_ready[bank], used + 1)
                    nc.vector.reciprocal(o_rcp[:, 0:HALF // 2], ps[:, 0:HALF // 2])
                elif name == "avg":
                    dve.wait_ge(side_ready[bank], used + 1)
                    if i == 0:
                        nc.vector.tensor_copy(g_mean[:], ps[:, 0:1]).then_inc(side_free[bank], 1)
                        dve.wait_ge(side_free[bank], used + 1)
                        nc.vector.tensor_tensor(g_diff[:], mv[:, 0:1], g_mean[:], ALU.subtract).then_inc(gn_step, 1)
                        dve.wait_ge(gn_step, b * 3 + 2)
                        nc.vector.scalar_tensor_tensor(g_sq[:], g_diff[:], g_diff[:], mv[:, 1:2],
                                                       ALU.mult, ALU.add).then_inc(gn_step, 1)
                    else:
                        nc.vector.tensor_scalar(g_var[:], ps[:, 0:1], GN_EPS, None, ALU.add).then_inc(side_free[bank], 1)
                return bank, used + 1

            def add_bottom(n, h):
                dve.wait_ge(bot, n * 2 + h + 1)
                for i in range(NH):
                    last = nc.vector.tensor_tensor(o_sum[D * i:D * i + D, :], ps_o[0:D, i * HALF:(i + 1) * HALF],
                                                   o_bot[D * i:D * i + D, :], ALU.add)
                last.then_inc(o_added, 1)

            def invert_rest(den):
                bank, _ = den
                nc.vector.reciprocal(o_rcp[:, HALF // 2:], side[bank][:, HALF // 2:]).then_inc(side_free[bank], 1)

            def normalise_out(n, h, inverted):
                dve.wait_ge(side_free[inverted[0]], inverted[1])
                dve.wait_ge(o_added, n * 2 + h + 1)
                for i in range(NH):
                    last = nc.vector.tensor_tensor(o_n[D * h:D * h + D, i * HALF:(i + 1) * HALF], o_sum[D * i:D * i + D, :],
                                                   o_rcp[D * i:D * i + D, :], ALU.mult)
                last.then_inc(o_norm, 1)

            third = CT // 2
            for i in range(PAIRS):
                part = slice(third * (i % 2), third * (i % 2 + 1))
                dve.wait_ge(w_hi_done, i + 1)
                if i >= 2:
                    dve.wait_ge(w_split_out[i % 2], 32 * (i // 2))
                nc.vector.tensor_tensor(xl[:, part, :], y[:, part, :], xh[:, part, :].bitcast(F32),
                                        ALU.subtract).then_inc(w_lo_done, 1)
                slot_statistics(0, i, i % 2, i // 2 + 1)
            for i in range(2):
                dve.wait_ge(w_split_out[i], 32 * (PAIRS // 2))

            dve.wait_ge(stats_done, CT)
            nc.vector.bn_aggr(mv[:], st[:]).then_inc(gn_step, 1)
            sides = sides_of(0, 0, "prologue")
            for tiles in PROLOGUE:
                for name, i in tiles:
                    read_side(sides, name, i, 0, 0, 0, 0)
                if tiles[0][0] == "avg":
                    for j in range(CT):
                        centre(0, j)
                        normalise_lo(0, j)

            def body(n, pair, b, kind):
                sides = sides_of(n, b, kind)
                state = {}

                def read_step(g, step):
                    for name, i in ended(step, CT):
                        if g < KT:
                            free = read_side(sides, name, i, 0, n, 1, b + 1)
                        else:
                            free = read_side(sides, name, i, 1, n + 1, 0, b + 1)
                        if name == "den":
                            state["den"] = free

                stats = kind == "loop" and not (isinstance(b, int) and b == B - 1)
                for g, step in enumerate(PLANS[kind]):
                    if kind == "last" and g == 0:
                        dve.wait_ge(stats_done, (b + 1) * PARTS + CT)
                    if g >= 1 and g - 1 not in POOL_LOWS:
                        probability_low(dve, nc.vector, n, g - 1)
                    elif g == 0 and kind != "start":
                        probability_low(dve, nc.vector, n - 1, STEPS - 1)
                    if g == 2 and kind != "start":
                        invert_rest(state["den"])
                        normalise_out(n - 1, 1, state["den"])
                    if g == KT + 2:
                        invert_rest(state["den"])
                        normalise_out(n, 0, state["den"])
                    if g == 1 and kind != "start":
                        add_bottom(n - 1, 1)
                    if g == KT + 1:
                        add_bottom(n, 0)
                    if kind == "last" and g == 0:
                        nc.vector.bn_aggr(mv[:], st[:]).then_inc(gn_step, 1)
                    if kind == "last" and 3 < g <= 3 + CT:
                        normalise_lo(b + 1, g - 4)
                    if kind == "last" and 3 <= g < 3 + CT:
                        centre(b + 1, g - 3)
                    read_step(g, step)
                    if stats and g == KT:
                        part_statistics(b + 1, pair - 1)

            loop(dve, body)
            n = B * PAIRS
            sides = sides_of(n, B - 1, "epilogue")
            probability_low(dve, nc.vector, n - 1, STEPS - 1)
            add_bottom(n - 1, 1)
            den = read_side(sides, "den", 1, 0, n, 1, 0)
            invert_rest(den)
            normalise_out(n - 1, 1, den)

        @block.tensor
        def _(pe):
            pe.wait_ge(consts_set, 5)
            pe.wait_ge(consts_in, 32)

            ready, newest = {}, {}

            def write_side(sides, piece, part, n, h, b, fresh_x):
                name, i, first, end = piece
                if first == 0:
                    bank, used = sides.next(name, i, part)
                    wait(pe, side_free[bank], used)
                    ready[name, i] = bank, used + 1
                    newest[bank] = name, i
                bank = ready[name, i][0]
                ps, half = side[bank], slice(i * HALF, (i + 1) * HALF)
                if name in ("qk", "v"):
                    w = wqk if name == "qk" else wv
                    if first == 0 and i == 0:
                        if name == "qk":
                            pe.wait_ge(wqk_in, 48 * (2 * n + h + 1))
                        else:
                            pe.wait_ge(wv_in, 48 * (n + 1))
                    for j in range(first, end):
                        if fresh_x and name == "qk" and i == 0:
                            pe.wait_ge(x_lo, b * CT + j + 1)
                        for k, (ww, xx) in enumerate(((w[0], xh), (w[0], xl), (w[1], xh))):
                            last = nc.tensor.matmul(ps[:], ww[:, j, :], xx[:, j, half], start=(j == 0 and k == 0),
                                                    stop=(j == CT - 1 and k == 2))
                elif name == "t":
                    for t in range(4):
                        last = nc.tensor.transpose(ps[:, t * P:(t + 1) * P], v_t[:, (4 * i + t) * P:(4 * i + t + 1) * P], ident[:])
                elif name == "max":
                    wait_ready(("qk", max(i // NH // 4, i % NH)))
                    t, keys = i // NH, slice((i % NH) * HALF, (i % NH + 1) * HALF)
                    last = nc.tensor.matmul(ps[:], qa[:, h, t * P:(t + 1) * P], ka[:, h, keys], start=True, stop=True)
                elif name == "turn":
                    if i == 0:
                        pe.wait_ge(max_done, 2 * n + h + 1)
                    for t in range(4):
                        last = nc.tensor.transpose(ps[0:1, t * P:(t + 1) * P], mx_row[:, 4 * i + t:4 * i + t + 1], ident[:])
                elif name == "den":
                    pe.wait_ge(p_sum, (n * 2 + h + 1) * (KT - 1))
                    for k in range(NH):
                        last = nc.tensor.matmul(ps[D * k:D * k + D, :], ones[:], sums[:, h, k * HALF:(k + 1) * HALF],
                                                start=True, stop=True)
                elif name == "avg":
                    pe.wait_ge(gn_step, b * 3 + 1 + 2 * i)
                    last = nc.tensor.matmul(ps[:, 0:1], gmean[:], mv[:, 0:1] if i == 0 else g_sq[:], start=True, stop=True)
                elif name == "out":
                    if i == OUT_ORDER[0]:
                        pe.wait_ge(wo_in, 32 * (n + 1))
                        pe.wait_ge(o_lo, n + 1)
                    j, cols = i // NH, slice((i % NH) * HALF, (i % NH + 1) * HALF)
                    for k, (ww, oo) in enumerate(((wo[0], oh), (wo[0], ol), (wo[1], oh))):
                        last = nc.tensor.matmul(ps[:], ww[:, j, :], oo[:, cols], start=(k == 0), stop=(k == 2))
                if end == CT:
                    last.then_inc(side_ready[bank], 1)

            def wait_ready(*tiles):
                for tile in tiles:
                    bank, count = ready[tile]
                    if newest[bank] == tile:
                        pe.wait_ge(side_free[bank], count)

            def score_step(n, g):
                h, t = g // KT, g % KT
                wait(pe, p_hi, n * STEPS + g)
                keys = slice(t * P, (t + 1) * P)
                for kk, qq, rows in ((ka, qa, P), (kb, qb, D + 1)):
                    for i in range(NH):
                        last = nc.tensor.matmul(ps_s[:, i * HALF:(i + 1) * HALF], kk[0:rows, h, keys],
                                                qq[0:rows, h, i * HALF:(i + 1) * HALF],
                                                start=(rows == P), stop=(rows != P))
                last.then_inc(scores, 1)

            def value_step(n, g):
                h, t = g // KT, g % KT
                if g in (0, KT // 2):
                    wait_ready(("t", t // 4))
                if t == 0:
                    wait(pe, o_added, n * 2 + h)
                pe.wait_ge(p_hi, n * STEPS + g + 1)
                for k, pp in enumerate((p_h, p_l)):
                    if k == 1:
                        pe.wait_ge(p_lo, n * STEPS + g + 1)
                    for i in range(NH):
                        last = nc.tensor.matmul(ps_o[:, i * HALF:(i + 1) * HALF], v[:, t, h, :],
                                                pp[:, g % 2, i * HALF:(i + 1) * HALF],
                                                start=(t == 0 and k == 0), stop=(t == KT - 1 and k == 1))
                last.then_inc(pv, 1)

            sides = sides_of(0, 0, "prologue")
            for tiles in PROLOGUE:
                for name, i in tiles:
                    write_side(sides, (name, i, 0, CT), 0, 0, 0, 0, True)

            def body(n, pair, b, kind):
                sides = sides_of(n, b, kind)

                def write_step(g, step):
                    k = g // KT
                    for piece in step:
                        name = piece[0]
                        if name == "avg":
                            write_side(sides, piece, k, n, 0, b + 1, False)
                        elif name == "den":
                            write_side(sides, piece, k, n - piece[1], piece[1], b, False)
                        elif name == "out":
                            write_side(sides, piece, k, n - 1, 0, b, False)
                        elif k == 0:
                            write_side(sides, piece, k, n, 1, b, False)
                        else:
                            write_side(sides, piece, k, n + 1, 0, b + 1, kind == "last")

                for g, step in enumerate(PLANS[kind]):
                    if g == 0:
                        for bank in TURN_BANKS:
                            pe.wait_ge(side_free[bank], sides.base[bank])
                    if g == KT:
                        wait_ready(("turn", 0), ("turn", 1))
                    score_step(n, g)
                    if g >= LAG:
                        value_step(n, g - LAG)
                    elif kind != "start":
                        value_step(n - 1, STEPS + g - LAG)
                    if g == 0:
                        pe.wait_ge(side_free[V_BANK], sides.base[V_BANK])
                    write_step(g, step)

            loop(pe, body)
            n = B * PAIRS
            sides = sides_of(n, B - 1, "epilogue")
            for g in range(STEPS - LAG, STEPS):
                value_step(n - 1, g)
            write_side(sides, ("den", 1, 0, CT), 0, n - 1, 1, B - 1, False)
            for i in OUT_ORDER:
                write_side(sides, ("out", i, 0, CT), 0, n - 1, 0, B - 1, False)


def kernel(x, L0_conv_in_proj_w, L0_conv_in_proj_b, L0_conv_out_proj_w, L0_conv_out_proj_b):
    import numpy as np
    import concourse.bacc as bacc
    from concourse.bass_utils import run_bass_kernel_spmd

    x = np.asarray(x)
    B, C, H, W = x.shape
    S, CT, PAIRS = H * W, C // P, C // P
    w_in = np.asarray(L0_conv_in_proj_w).reshape(3, PAIRS, 2, D, P, CT)
    w_qk = w_in[0:2].transpose(1, 4, 2, 5, 0, 3)
    w_qk = w_qk.reshape(PAIRS, P, 2 * CT * P)
    w_v = w_in[2].transpose(0, 3, 4, 1, 2).reshape(PAIRS, P, CT * P)
    w_out = np.asarray(L0_conv_out_proj_w).reshape(P, CT, PAIRS, P)
    w_out = w_out.transpose(2, 3, 1, 0).reshape(PAIRS, P, CT * P)
    b_in = np.asarray(L0_conv_in_proj_b).reshape(3, PAIRS, 2, D)
    b_qk = b_in[0:2].transpose(1, 2, 0, 3).reshape(PAIRS, 2, P)
    b_v = b_in[2].reshape(PAIRS, 1, P)
    arrays = {
        "x_dram": np.ascontiguousarray(x.reshape(B, C, S)),
        "w_all_dram": np.ascontiguousarray(np.concatenate([w_qk, w_v, w_out], axis=2)),
        "b_qkv_dram": np.ascontiguousarray(np.concatenate([b_qk, b_v], axis=1).reshape(PAIRS * 3, P, 1)),
        "b_out_dram": np.ascontiguousarray(np.asarray(L0_conv_out_proj_b).reshape(P, CT)),
        "group_mean_dram": np.kron(np.eye(GROUPS), np.full((P // GROUPS, P // GROUPS), GROUPS / P)).astype(np.float32),
    }
    nc = bacc.Bacc("TRN2", target_bir_lowering=False, num_devices=1)
    args = [nc.dram_tensor(n, a.shape, mybir.dt.from_np(a.dtype), kind="ExternalInput").ap() for n, a in arrays.items()]
    out = nc.dram_tensor("out_dram", (B, C, S), F32, kind="ExternalOutput").ap()
    conv_attention_kernel(nc, *args, out)
    r = run_bass_kernel_spmd(nc, [arrays], core_ids=[0])
    return r.results[0]["out_dram"].reshape(B, C, H, W)
```
